# Optimizing a Trainium2 kernel written in Bass

```python
import numpy as np
import jax
import jax.numpy as jnp

def _softmax(x, axis=-1):
    return jax.nn.softmax(x, axis=axis)

def _gelu(x):
    return jax.nn.gelu(x, approximate=True)

def _silu(x):
    return jax.nn.silu(x)

def _sigmoid(x):
    return jax.nn.sigmoid(x)

def _layernorm(x, axis=-1, eps=1e-05):
    m = jnp.mean(x, axis=axis, keepdims=True)
    v = jnp.var(x, axis=axis, keepdims=True)
    return (x - m) / jnp.sqrt(v + eps)

def _scatter_add(tgt, idx, src, axis=0):
    return tgt.at[idx].add(src)

def _segment_sum(src, seg, n):
    return jax.ops.segment_sum(src, seg, n)
kernel_name = 'mk_adj_resnorm_d1_adj_r2_d9d0b1'

def setup_inputs(seed: int=0):
    np.random.seed(seed)
    _w = jnp.asarray

    def _rec_inputs():
        import jax
        import jax.numpy as jnp
        _gk = jax.random.key(seed)
        x = -0.0005207 + 1.001 * jax.random.normal(jax.random.fold_in(_gk, 1), (8192, 128), jnp.float32)
        _a = jax.random.bernoulli(jax.random.fold_in(_gk, 2), 0.000488281, (8192, 8192))
        _a = jnp.logical_or(_a, jnp.swapaxes(_a, -1, -2))
        _a = jnp.logical_or(_a, jnp.eye(8192, dtype=bool))
        _af = _a.astype(jnp.float32)
        adj = _af
        return (x, adj)
    x, adj = _rec_inputs()

    def _L0_gnn_setup():
        import jax, jax.numpy as jnp
        import numpy as np
        NEG_INF = -9000000000000000.0
        NEG_SLOPE = 0.2
        key = jax.random.key(seed)
        k1, k2, k3, k4 = jax.random.split(key, 4)
        N, d_in, d_out = (4096, 128, 128)
        x = jax.random.normal(k1, (N, d_in), dtype=jnp.float32)
        adj = jax.random.randint(k2, (N, N), 0, 2).astype(jnp.float32)
        W = jax.random.normal(k3, (d_in, d_out), dtype=jnp.float32) * (1.0 / np.sqrt(d_in))
        a = jax.random.normal(k4, (2 * d_out,), dtype=jnp.float32) * (1.0 / np.sqrt(2 * d_out))
        return {'x': x, 'adj': adj, 'W': W, 'a': a}
    _L0_gnn_all = _L0_gnn_setup()
    _L0_gnn_in = {k: v for k, v in _L0_gnn_all.items() if k in ('W', 'a')}
    del _L0_gnn_all
    return {'x': x, 'adj': adj, 'L0_gnn_W': _L0_gnn_in['W'], 'L0_gnn_a': _L0_gnn_in['a']}

def reference(x, adj, L0_gnn_W, L0_gnn_a):
    import jax
    import jax.numpy as jnp

    def _L0_gnn_ref(x, adj, W, a):
        import jax, jax.numpy as jnp
        import numpy as np
        NEG_INF = -9000000000000000.0
        NEG_SLOPE = 0.2
        d_out = W.shape[1]
        Wh = x @ W
        e_src = Wh @ a[:d_out]
        e_dst = Wh @ a[d_out:]
        e = jax.nn.leaky_relu(e_src[:, None] + e_dst[None, :], NEG_SLOPE)
        N = Wh.shape[0]
        mask = (adj > 0) | jnp.eye(N, dtype=bool)
        e = jnp.where(mask, e, NEG_INF)
        alpha = jax.nn.softmax(e, axis=1)
        h = alpha @ Wh
        return h
    x = _layernorm(x + _L0_gnn_ref(x, adj, L0_gnn_W, L0_gnn_a), axis=-1)
    return x

_drawn_inputs = setup_inputs


def setup_inputs(seed=0):
    import zlib

    import numpy as np

    out = dict(_drawn_inputs(seed))
    spreads = {}
    factors = {}
    for name, (base, spread) in spreads.items():
        noise = np.random.default_rng([zlib.crc32(name.encode()), seed]).standard_normal(out[name].shape)
        drawn = base * np.exp(spread * noise) if base else spread * noise
        out[name] = jnp.asarray(drawn.astype(out[name].dtype))
    for name, factor in factors.items():
        out[name] = (out[name] * factor).astype(out[name].dtype)
    return out
```

```python
import concourse.bass as bass
from concourse import mybir
from contextlib import ExitStack


def gat_resnorm_kernel(nc: bass.Bass, x_dram: bass.AP, adj_dram: bass.AP, w_dram: bass.AP, a_dram: bass.AP,
                       out_dram: bass.AP):
    fp32 = mybir.dt.float32
    bf16 = mybir.dt.bfloat16
    i32 = mybir.dt.int32
    ALU = mybir.AluOpType
    ACT = mybir.ActivationFunctionType
    AX = mybir.AxisListType

    P = 128
    N, D = x_dram.shape
    SLOPE = 0.2
    EPS = 1e-5
    RT = N // P
    G = 4
    GR = G * P
    NG = RT // G
    CH = 1024
    CT = CH // P
    NC = N // CH
    PAIR = 2 * CT
    NP = NC // 2
    AR = 4
    MR = 2
    TR = 4
    PR = 4
    LEAD = TR - 1
    XR = 4
    DE = D + 1
    RQ = 4

    x_rows = x_dram.rearrange("(t p) d -> p t d", p=P)
    out_rows = out_dram.rearrange("(t p) d -> p t d", p=P)
    adj_rows = adj_dram.rearrange("(t p) j -> p t j", p=P)
    adj_diag = bass.AP(tensor=adj_dram.tensor, offset=0, ap=[[N + 1, P], [P * (N + 1), RT], [1, 1]])

    ctx = ExitStack()
    with ctx:
        def sb(name, shape, dt):
            return ctx.enter_context(nc.sbuf_tensor(name, shape, dt))

        def sem(name):
            return ctx.enter_context(nc.semaphore(name))

        adj_sb = sb("adj_sb", [P, AR, G, CH], fp32)
        mask_sb = sb("mask_sb", [P, MR, G, CH], bf16)
        rho = sb("rho", [P, N], fp32)
        whv = sb("whv", [P, RT, D + 2], fp32)
        pt = sb("pt", [P, PR, GR], fp32)
        x_in_sb = sb("x_in_sb", [P, XR, G, D], fp32)
        x_res = sb("x_res", [P, G, D], fp32)
        xt = sb("xt", [P, 2, GR], fp32)
        w_ext = sb("w_ext", [P, D + 2], fp32)
        wt = sb("wt", [P, D], fp32)
        a_sb = sb("a_sb", [P, 2], fp32)
        wsrc_rep = sb("wsrc_rep", [P, P], fp32)
        ident = sb("ident", [P, P], fp32)
        ident_b = sb("ident_b", [P, P], bf16)
        st = sb("st", [P, 2, RT], fp32)
        tmax_p = sb("tmax_p", [P, 1], fp32)
        tmax = sb("tmax", [P, 1], fp32)
        shift8 = sb("shift8", [P, 1], fp32)
        shift2 = sb("shift2", [P, 1], fp32)
        q = sb("q", [P, RT], fp32)
        v = sb("v", [P, RT], fp32)
        rho_col = sb("rho_col", [P, RT], fp32)
        diag = sb("diag", [P, RT, 1], fp32)
        top = sb("top", [P, RT], fp32)
        self_num = sb("self_num", [P, RT], fp32)
        num = sb("num", [P, G, DE], fp32)
        rden = sb("rden", [P, G], fp32)
        y = sb("y", [P, G, D], fp32)
        stats = sb("stats", [P, G, 6], fp32)
        mv = sb("mv", [P, G, 2], fp32)
        eps_sb = sb("eps_sb", [P, 1], fp32)
        std = sb("std", [P, G], fp32)
        rstd = sb("rstd", [P, G], fp32)
        o_sb = sb("o_sb", [P, G, D], fp32)

        tr = [ctx.enter_context(nc.psum_tensor(f"tr{k}", [P, 512], fp32)) for k in range(TR)]
        acc = [ctx.enter_context(nc.psum_tensor(f"acc{a}", [P, 512], fp32)) for a in range(G)]
        tr_b = [t[:, :].bitcast(bf16)[:, 0:GR] for t in tr]

        x_in = [sem(f"x_in{k}") for k in range(XR)]
        w_in = sem("w_in")
        a_in = sem("a_in")
        diag_in = sem("diag_in")
        x_res_in = sem("x_res_in")
        adj_in = [sem(f"adj_in{k}") for k in range(AR)]
        zeroed = sem("zeroed")
        idents_ready = sem("idents_ready")
        consts_ready = sem("consts_ready")
        wt_psum = sem("wt_psum")
        wt_ready = sem("wt_ready")
        wa_psum = sem("wa_psum")
        wa_ready = sem("wa_ready")
        wext_ready = sem("wext_ready")
        xt_psum = sem("xt_psum")
        xt_ready = sem("xt_ready")
        wh_psum = sem("wh_psum")
        srow_psum = sem("srow_psum")
        srow_ready = sem("srow_ready")
        st_ready = sem("st_ready")
        tmaxp_ready = sem("tmaxp_ready")
        tmax_ready = sem("tmax_ready")
        shift_ready = sem("shift_ready")
        qv_ready = sem("qv_ready")
        rhocol_exp = sem("rhocol_exp")
        rho_exp = sem("rho_exp")
        self_step = sem("self_step")
        ones_ready = sem("ones_ready")
        rho_ready = sem("rho_ready")
        whv_ready = sem("whv_ready")
        mask_ready = sem("mask_ready")
        tr_ready = sem("tr_ready")
        pt_ready = sem("pt_ready")
        pt_used = sem("pt_used")
        acc_ready = sem("acc_ready")
        acc_taken = sem("acc_taken")
        rden_ready = sem("rden_ready")
        y_ready = sem("y_ready")
        stats_ready = sem("stats_ready")
        var_ready = sem("var_ready")
        std_ready = sem("std_ready")
        rstd_ready = sem("rstd_ready")
        o_ready = sem("o_ready")
        o_out = sem("o_out")

        block = ctx.enter_context(nc.Block())

        @block.sync
        def _(sp):
            def load_x(g, k):
                sp.dma_start(x_in_sb[:, k, :, :], x_rows[:, bass.ds(g * G + k * G, G), :]).then_inc(x_in[k], 16)

            def load_adj(g, c):
                sp.dma_start(adj_sb[:, c % AR, :, :],
                             adj_rows[:, bass.ds(g * G, G), c * CH:(c + 1) * CH]).then_inc(adj_in[c % AR], 16)

            for k in range(XR):
                load_x(0, k)
            with sp.Fori(1, NG // XR) as b:
                for k in range(XR):
                    sp.wait_ge(xt_psum, b * XR + (k - XR + 1))
                    load_x(b * XR, k)
            def load_residual(g):
                sp.dma_start(x_res[:, :, :], x_rows[:, bass.ds(g * G, G), :]).then_inc(x_res_in, 16)

            def store(g):
                sp.wait_ge(o_ready, g + 1)
                sp.dma_start(out_rows[:, bass.ds(g * G, G), :], o_sb[:, :, :]).then_inc(o_out, 16)
                sp.wait_ge(o_out, g * 16 + 16)

            for c in range(NC):
                if c >= AR:
                    sp.wait_ge(mask_ready, c - AR + 1)
                load_adj(0, c)
            load_residual(0)
            with sp.Fori(1, NG) as g:
                for c in range(NC):
                    sp.wait_ge(mask_ready, g * NC + (c - AR + 1))
                    load_adj(g, c)
                store(g - 1)
                load_residual(g)
            store(NG - 1)

        @block.gpsimd
        def _(pool):
            nc.gpsimd.memset(ident[:, :], 0.0)
            nc.gpsimd.memset(ident_b[:, :], 0.0).then_inc(zeroed, 1)
            pool.wait_ge(zeroed, 1)
            nc.gpsimd.affine_select(out=ident[:, :], in_=ident[:, :], compare_op=ALU.not_equal, fill=1.0, base=0,
                                    pattern=[[-1, P]], channel_multiplier=1)
            nc.gpsimd.affine_select(out=ident_b[:, :], in_=ident_b[:, :], compare_op=ALU.not_equal, fill=1.0, base=0,
                                    pattern=[[-1, P]], channel_multiplier=1).then_inc(idents_ready, 1)
            with nc.allow_non_contiguous_dma(reason="the diagonal of adj"):
                pool.dma_start(diag[:, :, :], adj_diag).then_inc(diag_in, 16)
            pool.wait_ge(tmaxp_ready, 1)
            nc.gpsimd.partition_all_reduce(tmax[:, :], tmax_p[:, :], P,
                                           bass.bass_isa.ReduceOp.max).then_inc(tmax_ready, 1)

        @block.scalar
        def _(act):
            act.dma_start(w_ext[:, 0:D], w_dram).then_inc(w_in, 16)
            with nc.allow_non_contiguous_dma(reason="a_src and a_dst as columns"):
                act.dma_start(a_sb[:, :], a_dram.rearrange("(k p) -> p k", p=P)).then_inc(a_in, 16)
            act.wait_ge(wt_psum, 1)
            nc.scalar.copy(wt[:, :], tr[0][:, 0:D]).then_inc(wt_ready, 1)

            def copy_xt(g, k):
                act.wait_ge(xt_psum, g + (k + 1))
                if not isinstance(g, int) or k >= 2:
                    act.wait_ge(srow_psum, g + (k - 1))
                nc.scalar.copy(xt[:, k % 2, :], tr[k % 2][:, :]).then_inc(xt_ready, 1)

            def copy_srow(g, k):
                act.wait_ge(srow_psum, g + (k + 1))
                nc.scalar.copy(rho[:, bass.ds(g * GR + k * GR, GR)], tr[2 + k % 2][:, :]).then_inc(srow_ready, 1)

            copy_xt(0, 0)
            copy_xt(0, 1)
            with act.Fori(0, NG // 2 - 1) as b:
                for k in range(2):
                    copy_srow(b * 2, k)
                    copy_xt(b * 2, k + 2)
            copy_srow(NG - 2, 0)
            copy_srow(NG - 2, 1)
            act.wait_ge(shift_ready, 1)
            act.wait_ge(st_ready, 1)
            nc.scalar.activation(q[:, :], st[:, 1, :], ACT.Exp, bias=shift8[:, :], scale=1.0 - SLOPE)
            nc.scalar.activation(v[:, :], st[:, 1, :], ACT.Exp, bias=shift2[:, :], scale=SLOPE).then_inc(qv_ready, 1)
            act.wait_ge(srow_ready, NG)
            for k in range(RQ):
                r = slice(k * N // RQ, (k + 1) * N // RQ)
                nc.scalar.activation(rho[:, r], rho[:, r], ACT.Exp, bias=shift8[:, :],
                                     scale=-(1.0 - SLOPE)).then_inc(rho_exp, 1)
            nc.scalar.activation(rho_col[:, :], st[:, 0, :], ACT.Exp, bias=shift8[:, :],
                                 scale=-(1.0 - SLOPE)).then_inc(rhocol_exp, 1)

            def mask(g, c, first):
                act.wait_ge(adj_in[c % AR], g * (16 * NC // AR) + 16 * (c // AR + 1))
                if not (first and c < MR):
                    act.wait_ge(tr_ready, g * RT + (c - MR + 1) * CT)
                nc.scalar.activation(mask_sb[:, c % MR, :, :], adj_sb[:, c % AR, :, :].bitcast(i32),
                                     ACT.Relu).then_inc(mask_ready, 1)

            def std_of(g):
                act.wait_ge(var_ready, g + 1)
                nc.scalar.activation(std[:, :], mv[:, :, 1], ACT.Sqrt, bias=eps_sb[:, :]).then_inc(std_ready, 1)

            act.wait_ge(consts_ready, 1)
            for c in range(NC):
                mask(0, c, True)
            with act.Fori(1, NG) as g:
                for c in range(NC):
                    mask(g, c, False)
                    if c == 2:
                        std_of(g - 1)
            std_of(NG - 1)

        @block.vector
        def _(dve):
            nc.vector.memset(eps_sb[:, :], EPS).then_inc(consts_ready, 1)
            dve.wait_ge(w_in, 16)
            dve.wait_ge(wa_psum, 1)
            nc.vector.tensor_copy(w_ext[:, D:D + 2], acc[0][:, 0:2]).then_inc(wa_ready, 1)
            dve.wait_ge(wa_ready, 1)
            nc.vector.tensor_copy(wsrc_rep[:, :], w_ext[:, D:D + 1].broadcast_to([P, P])).then_inc(wext_ready, 1)
            with dve.Fori(0, NG) as g:
                for a in range(G):
                    dve.wait_ge(wh_psum, g * G + (a + 1))
                    nc.vector.tensor_copy(whv[:, bass.ds(g * G + a, 1), :].rearrange("p t d -> p (t d)"),
                                          acc[a][:, 0:D + 2]).then_inc(acc_taken, 1)
            dve.wait_ge(acc_taken, RT)
            nc.vector.reduce_max(tmax_p[:, :], whv[:, :, D + 1], AX.X).then_inc(tmaxp_ready, 1)
            nc.vector.tensor_copy(st[:, :, :], whv[:, :, D:D + 2].rearrange("p t k -> p k t")).then_inc(st_ready, 1)
            dve.wait_ge(st_ready, 1)
            nc.vector.memset(whv[:, :, D:D + 1], 1.0).then_inc(ones_ready, 1)
            dve.wait_ge(tmax_ready, 1)
            nc.vector.tensor_scalar(shift8[:, :], tmax[:, :], -(1.0 - SLOPE), None, ALU.mult)
            nc.vector.tensor_scalar(shift2[:, :], tmax[:, :], -SLOPE, None, ALU.mult).then_inc(shift_ready, 1)
            dve.wait_ge(qv_ready, 1)
            dve.wait_ge(ones_ready, 1)
            nc.vector.tensor_tensor(whv[:, :, 0:DE], whv[:, :, 0:DE], v[:, :].unsqueeze(2).broadcast_to([P, RT, DE]),
                                    ALU.mult).then_inc(whv_ready, 1)
            for k in range(RQ):
                dve.wait_ge(rho_exp, k + 1)
                r = slice(k * N // RQ, (k + 1) * N // RQ)
                nc.vector.tensor_scalar(rho[:, r], rho[:, r], 1.0, None, ALU.min).then_inc(rho_ready, 1)
            dve.wait_ge(rhocol_exp, 1)
            nc.vector.tensor_scalar(rho_col[:, :], rho_col[:, :], 1.0, None, ALU.min).then_inc(self_step, 1)
            dve.wait_ge(self_step, 1)
            nc.vector.tensor_tensor(top[:, :], rho_col[:, :], q[:, :], ALU.max).then_inc(self_step, 1)
            dve.wait_ge(self_step, 2)
            dve.wait_ge(diag_in, 16)
            nc.vector.scalar_tensor_tensor(out=self_num[:, :], in0=diag[:, :, 0], scalar=0.0, in1=top[:, :],
                                           op0=ALU.is_le, op1=ALU.mult).then_inc(self_step, 1)
            dve.wait_ge(self_step, 3)
            dve.wait_ge(rho_ready, RQ)

            def numerators(g, p, k, first):
                n = g * RT + p * PAIR + k
                dve.wait_ge(tr_ready, n + 1)
                if not (first and k < PR):
                    dve.wait_ge(pt_used, n - (PR - 1))
                nc.vector.scalar_tensor_tensor(
                    out=pt[:, k % PR, :], in0=rho[:, bass.ds(g * GR, GR)], scalar=q[:, bass.ds(p * PAIR + k, 1)],
                    in1=tr_b[k % TR], op0=ALU.max, op1=ALU.min).then_inc(pt_ready, 1)

            def take_sums(g):
                for a in range(G):
                    dve.wait_ge(acc_ready, g * G + (a + 1))
                    nc.vector.scalar_tensor_tensor(
                        out=num[:, a, :], in0=whv[:, bass.ds(g * G + a, 1), 0:DE].rearrange("p t d -> p (t d)"),
                        scalar=self_num[:, bass.ds(g * G + a, 1)], in1=acc[a][:, 0:DE],
                        op0=ALU.mult, op1=ALU.add).then_inc(acc_taken, 1)

            def invert_denominators(g):
                dve.wait_ge(acc_taken, g * G + (RT + G))
                nc.vector.reciprocal(rden[:, :], num[:, :, D]).then_inc(rden_ready, 1)

            def add_residual(g):
                dve.wait_ge(rden_ready, g + 1)
                dve.wait_ge(x_res_in, g * 16 + 16)
                for a in range(G):
                    nc.vector.scalar_tensor_tensor(out=y[:, a, :], in0=num[:, a, 0:D], scalar=rden[:, a:a + 1],
                                                   in1=x_res[:, a, :], op0=ALU.mult, op1=ALU.add).then_inc(y_ready, 1)

            def row_stats(g):
                for a in range(G):
                    dve.wait_ge(y_ready, g * G + (a + 1))
                    last = nc.vector.bn_stats(stats[:, a, :], y[:, a, :])
                last.then_inc(stats_ready, 1)

            def row_variances():
                for a in range(G):
                    last = nc.vector.bn_aggr(mv[:, a, :], stats[:, a, :])
                last.then_inc(var_ready, 1)

            def invert_std(g):
                dve.wait_ge(std_ready, g + 1)
                nc.vector.reciprocal(rstd[:, :], std[:, :]).then_inc(rstd_ready, 1)

            def normalise(g):
                dve.wait_ge(rstd_ready, g + 1)
                dve.wait_ge(var_ready, g + 1)
                for a in range(G):
                    last = nc.vector.tensor_scalar(o_sb[:, a, :], y[:, a, :], mv[:, a, 0:1], rstd[:, a:a + 1],
                                                   ALU.subtract, ALU.mult)
                last.then_inc(o_ready, 1)

            def pair(g, p, first):
                for k in range(PAIR):
                    numerators(g, p, k, first)

            pair(0, 0, True)
            with dve.Fori(1, NP) as p:
                pair(0, p, False)
            with dve.Fori(1, NG) as g:
                for k in range(PAIR):
                    if k == 8:
                        dve.wait_ge(stats_ready, g)
                    numerators(g, 0, k, False)
                    if k == 2:
                        take_sums(g - 1)
                    elif k == 3:
                        invert_denominators(g - 1)
                    elif k == 4:
                        add_residual(g - 1)
                    elif k == 6:
                        row_stats(g - 1)
                    elif k == 8:
                        row_variances()
                    elif k == PAIR - 2:
                        invert_std(g - 1)
                    elif k == PAIR - 1:
                        normalise(g - 1)
                with dve.Fori(1, NP) as p:
                    pair(g, p, False)
            take_sums(NG - 1)
            invert_denominators(NG - 1)
            add_residual(NG - 1)
            row_stats(NG - 1)
            dve.wait_ge(stats_ready, NG)
            row_variances()
            invert_std(NG - 1)
            normalise(NG - 1)

        @block.tensor
        def _(pe):
            pe.wait_ge(idents_ready, 1)
            pe.wait_ge(w_in, 16)
            nc.tensor.transpose(tr[0][:, 0:D], w_ext[:, 0:D], ident[:, :]).then_inc(wt_psum, 1)
            pe.wait_ge(wt_ready, 1)
            pe.wait_ge(a_in, 16)
            nc.tensor.matmul(acc[0][:, 0:2], wt[:, :], a_sb[:, :], start=True, stop=True).then_inc(wa_psum, 1)
            pe.wait_ge(wext_ready, 1)

            def transpose_x(b, k, first=False):
                g = b * XR
                pe.wait_ge(x_in[k % XR], b * 16 + 16 * (k // XR + 1))
                if not (first and k < 2):
                    pe.wait_ge(xt_ready, g + (k - 1))
                for a in range(G):
                    last = nc.tensor.transpose(tr[k % 2][:, a * P:(a + 1) * P], x_in_sb[:, k % XR, a, :], ident[:, :])
                last.then_inc(xt_psum, 1)

            def project_x(b, k, first=False):
                g = b * XR
                pe.wait_ge(xt_ready, g + (k + 1))
                for a in range(G):
                    if not (first and k == 0):
                        pe.wait_ge(acc_taken, (g + (k - 1)) * G + (a + 1))
                    nc.tensor.matmul(acc[a][:, 0:D + 2], xt[:, k % 2, a * P:(a + 1) * P], w_ext[:, :],
                                     start=True, stop=True).then_inc(wh_psum, 1)
                if not (first and k < 2):
                    pe.wait_ge(srow_ready, g + (k - 1))
                nc.tensor.matmul(tr[2 + k % 2][:, :], wsrc_rep[:, :], xt[:, k % 2, :],
                                 start=True, stop=True).then_inc(srow_psum, 1)

            NB = NG // XR
            transpose_x(0, 0, True)
            for k in range(XR):
                transpose_x(0, k + 1, True)
                project_x(0, k, True)
            with pe.Fori(1, NB - 1) as b:
                for k in range(XR):
                    transpose_x(b, k + 1)
                    project_x(b, k)
            for k in range(XR):
                if k + 1 < XR:
                    transpose_x(NB - 1, k + 1)
                project_x(NB - 1, k)

            def transpose_mask(g, p, k):
                pe.wait_ge(mask_ready, g * NC + p * 2 + (k // CT + 1))
                for a in range(G):
                    last = nc.tensor.transpose(tr_b[k % TR][:, a * P:(a + 1) * P],
                                               mask_sb[:, (k // CT) % MR, a, (k % CT) * P:(k % CT + 1) * P],
                                               ident_b[:, :])
                last.then_inc(tr_ready, 1)

            def pair(g, p, first, last, final):
                for k in range(PAIR):
                    n = g * RT + p * PAIR + k
                    if k + LEAD < PAIR or not final:
                        transpose_mask(g, p, k + LEAD)
                    pe.wait_ge(pt_ready, n + 1)
                    for a in range(G):
                        if first and k == 0:
                            pe.wait_ge(acc_taken, (g - 1) * G + (RT + a + 1))
                        mm = nc.tensor.matmul(
                            acc[a][:, 0:DE], pt[:, k % PR, a * P:(a + 1) * P],
                            whv[:, bass.ds(p * PAIR + k, 1), 0:DE].rearrange("p t d -> p (t d)"),
                            start=first and k == 0, stop=last and k == PAIR - 1)
                        if last and k == PAIR - 1:
                            mm.then_inc(acc_ready, 1)
                        elif a == G - 1:
                            mm.then_inc(pt_used, 1)
                    if last and k == PAIR - 1:
                        pe.wait_ge(acc_ready, (g + 1) * G)
                        pe.sem_inc(pt_used, 1)

            pe.wait_ge(xt_ready, NG)
            pe.wait_ge(srow_ready, NG)
            for k in range(LEAD):
                transpose_mask(0, 0, k)
            pe.wait_ge(whv_ready, 1)
            with pe.Fori(0, NG - 1) as g:
                pair(g, 0, True, False, False)
                with pe.Fori(1, NP - 1) as p:
                    pair(g, p, False, False, False)
                pair(g, NP - 1, False, True, False)
            pair(NG - 1, 0, True, False, False)
            with pe.Fori(1, NP - 1) as p:
                pair(NG - 1, p, False, False, False)
            pair(NG - 1, NP - 1, False, True, True)


_INS = ["x", "adj", "L0_gnn_W", "L0_gnn_a"]
_OUTS = [((8192, 128), "float32")]


def kernel(**inputs):
    import numpy as _np
    import concourse.bacc as _bacc
    from concourse import mybir as _mybir
    from concourse.bass_utils import run_bass_kernel_spmd as _run

    nc = _bacc.Bacc("TRN2", target_bir_lowering=False, num_devices=1)
    arrays, args = {}, []
    for name in _INS:
        a = _np.ascontiguousarray(inputs[name])
        arrays[f"in_{name}_dram"] = a
        args.append(nc.dram_tensor(f"in_{name}_dram", a.shape, _mybir.dt.from_np(a.dtype), kind="ExternalInput").ap())
    for i, (shape, dtype) in enumerate(_OUTS):
        dt = _mybir.dt.from_np(_np.dtype(dtype))
        args.append(nc.dram_tensor(f"out_{i}_dram", shape, dt, kind="ExternalOutput").ap())
    gat_resnorm_kernel(nc, *args)
    r = _run(nc, [arrays], core_ids=[0])
    return r.results[0]["out_0_dram"]
```

```python
import concourse.bass as bass
from concourse import mybir
from contextlib import ExitStack


def gat_resnorm_kernel(nc: bass.Bass, x_dram: bass.AP, adj_dram: bass.AP, w_dram: bass.AP, a_dram: bass.AP,
                       out_dram: bass.AP):
    fp32 = mybir.dt.float32
    i32 = mybir.dt.int32
    u8 = mybir.dt.uint8
    ALU = mybir.AluOpType
    ACT = mybir.ActivationFunctionType
    AX = mybir.AxisListType

    P = 128
    N, D = x_dram.shape
    SLOPE = 0.2
    EPS = 1e-5
    RT = N // P
    G = 4
    GR = G * P
    NG = RT // G
    CH = 1024
    CT = CH // P
    NC = N // CH
    PAIR = 2 * CT
    NP = NC // 2
    AR = 4
    MR = 2
    PK = 4
    TR = 2
    PR = 4
    LEAD = TR - 1
    BC = CT // PK
    XT = 4
    X_PIECES = [0, 1, 2, 4, 8, NG]
    DE = D + 1
    VC = 8
    RHO_AT = 8
    MASK_SCALE = 2.0 ** -23

    x_tiles = x_dram.rearrange("(g p a) d -> p g a d", p=P, a=G)
    out_tiles = out_dram.rearrange("(g p a) d -> p g a d", p=P, a=G)
    adj_tiles = adj_dram.rearrange("(g p a) j -> p g a j", p=P, a=G)

    ctx = ExitStack()
    with ctx:
        def sb(name, shape, dt):
            return ctx.enter_context(nc.sbuf_tensor(name, shape, dt))

        def sem(name):
            return ctx.enter_context(nc.semaphore(name))

        adj_sb = sb("adj_sb", [P, AR, G, CH], fp32)
        mask_sb = sb("mask_sb", [P, MR, G, CH], u8)
        rho = sb("rho", [P, GR], fp32)
        whv = sb("whv", [P, RT, D + 2], fp32)
        pt = sb("pt", [P, PR, GR], fp32)
        x_sb = sb("x_sb", [P, NG, G, D], fp32)
        xt = sb("xt", [P, XT, GR], fp32)
        w_ext = sb("w_ext", [P, D + 2], fp32)
        wt = sb("wt", [P, D], fp32)
        a_sb = sb("a_sb", [P, 2], fp32)
        ident = sb("ident", [P, P], fp32)
        st = sb("st", [P, 2, RT], fp32)
        tmax_p = sb("tmax_p", [P, 1], fp32)
        tmax = sb("tmax", [P, 1], fp32)
        shift8 = sb("shift8", [P, 1], fp32)
        shift2 = sb("shift2", [P, 1], fp32)
        q = sb("q", [P, RT], fp32)
        v = sb("v", [P, RT], fp32)
        rho_col = sb("rho_col", [P, RT], fp32)
        rho_next = sb("rho_next", [P, G], fp32)
        diag = sb("diag", [P, NG, G, 1], fp32)
        top = sb("top", [P, RT], fp32)
        self_num = sb("self_num", [P, RT], fp32)
        num = sb("num", [P, G, DE], fp32)
        rden = sb("rden", [P, G], fp32)
        y = sb("y", [P, G, D], fp32)
        stats = sb("stats", [P, G, 6], fp32)
        mv = sb("mv", [P, G, 2], fp32)
        eps_sb = sb("eps_sb", [P, 1], fp32)
        std = sb("std", [P, G], fp32)
        rstd = sb("rstd", [P, G], fp32)
        o_sb = sb("o_sb", [P, G, D], fp32)

        tr = [ctx.enter_context(nc.psum_tensor(f"tr{k}", [P, 512], fp32)) for k in range(TR)]
        acc = [ctx.enter_context(nc.psum_tensor(f"acc{a}", [P, 512], fp32)) for a in range(G)]
        rho_ps = ctx.enter_context(nc.psum_tensor("rho_ps", [P, 512], fp32))
        tr_mask = [[t[:, :].bitcast(u8).rearrange("p (i h) -> p i h", h=PK)[:, :, h] for h in range(PK)] for t in tr]

        x_in = [sem(f"x_in{k}") for k in range(len(X_PIECES) - 1)]
        w_in = sem("w_in")
        a_in = sem("a_in")
        diag_in = sem("diag_in")
        adj_in = [sem(f"adj_in{k}") for k in range(AR)]
        zeroed = sem("zeroed")
        ident_ready = sem("ident_ready")
        consts_ready = sem("consts_ready")
        wt_psum = sem("wt_psum")
        wt_ready = sem("wt_ready")
        wa_psum = sem("wa_psum")
        wext_ready = sem("wext_ready")
        xt_psum = sem("xt_psum")
        xt_ready = sem("xt_ready")
        wh_psum = sem("wh_psum")
        st_ready = sem("st_ready")
        tmaxp_ready = sem("tmaxp_ready")
        tmax_ready = sem("tmax_ready")
        shift_ready = sem("shift_ready")
        v_ready = sem("v_ready")
        q_ready = sem("q_ready")
        rhocol_exp = sem("rhocol_exp")
        rhocol_ready = sem("rhocol_ready")
        self_step = sem("self_step")
        ones_ready = sem("ones_ready")
        whv_ready = sem("whv_ready")
        rho_next_ready = sem("rho_next_ready")
        rho_psum = sem("rho_psum")
        rho_ready = sem("rho_ready")
        mask_ready = sem("mask_ready")
        tr_ready = sem("tr_ready")
        pt_ready = sem("pt_ready")
        pt_used = sem("pt_used")
        acc_ready = sem("acc_ready")
        acc_taken = sem("acc_taken")
        rden_ready = sem("rden_ready")
        y_ready = sem("y_ready")
        stats_ready = sem("stats_ready")
        var_ready = sem("var_ready")
        std_ready = sem("std_ready")
        rstd_ready = sem("rstd_ready")
        o_ready = sem("o_ready")
        o_out = sem("o_out")

        block = ctx.enter_context(nc.Block())

        @block.sync
        def _(sp):
            def load_adj(g, c):
                sp.dma_start(adj_sb[:, c % AR, :, :],
                             adj_tiles[:, bass.ds(g, 1), :, c * CH:(c + 1) * CH]).then_inc(adj_in[c % AR], 16)

            def store(g):
                sp.wait_ge(o_ready, g + 1)
                sp.dma_start(out_tiles[:, bass.ds(g, 1), :, :], o_sb[:, :, :]).then_inc(o_out, 16)

            for k in range(len(X_PIECES) - 1):
                r = slice(X_PIECES[k], X_PIECES[k + 1])
                sp.dma_start(x_sb[:, r, :, :], x_tiles[:, r, :, :]).then_inc(x_in[k], 16)
            for c in range(NC):
                if c >= AR:
                    sp.wait_ge(mask_ready, (c - AR + 1) * G)
                load_adj(0, c)
            with sp.Fori(1, NG) as g:
                for c in range(NC):
                    sp.wait_ge(mask_ready, g * (NC * G) + (c - AR + 1) * G)
                    load_adj(g, c)
                store(g - 1)
            store(NG - 1)
            sp.wait_ge(o_out, 16 * NG)

        @block.gpsimd
        def _(pool):
            nc.gpsimd.memset(ident[:, :], 0.0).then_inc(zeroed, 1)
            pool.wait_ge(zeroed, 1)
            nc.gpsimd.affine_select(out=ident[:, :], in_=ident[:, :], compare_op=ALU.not_equal, fill=1.0, base=0,
                                    pattern=[[-1, P]], channel_multiplier=1).then_inc(ident_ready, 1)
            with nc.allow_non_contiguous_dma(reason="the diagonal of adj"):
                for a in range(G):
                    pool.dma_start(diag[:, :, a, :],
                                   bass.AP(tensor=adj_dram.tensor, offset=a * (N + 1),
                                           ap=[[G * (N + 1), P], [GR * (N + 1), NG], [1, 1]])).then_inc(diag_in, 16)
            pool.wait_ge(tmaxp_ready, 1)
            nc.gpsimd.partition_all_reduce(tmax[:, :], tmax_p[:, :], P,
                                           bass.bass_isa.ReduceOp.max).then_inc(tmax_ready, 1)
            pool.wait_ge(acc_taken, RT)
            pool.wait_ge(ones_ready, 1)
            pool.wait_ge(v_ready, 1)
            for k in range(0, RT, VC):
                piece = whv[:, k:k + VC, 0:DE]
                nc.gpsimd.tensor_tensor(piece, piece, v[:, k:k + VC].unsqueeze(2).broadcast_to([P, VC, DE]),
                                        ALU.mult).then_inc(whv_ready, 1)

        @block.scalar
        def _(act):
            act.dma_start(w_ext[:, 0:D], w_dram).then_inc(w_in, 16)
            with nc.allow_non_contiguous_dma(reason="a_src and a_dst as columns"):
                act.dma_start(a_sb[:, :], a_dram.rearrange("(k p) -> p k", p=P)).then_inc(a_in, 16)
            def copy_xt(g):
                act.wait_ge(xt_psum, g + 1)
                if g >= XT:
                    act.wait_ge(wh_psum, (g - XT + 1) * G)
                nc.scalar.copy(xt[:, g % XT, :], tr[g % TR][:, :]).then_inc(xt_ready, 1)

            for g in range(NG - G):
                copy_xt(g)
            act.wait_ge(adj_in[0], 16)
            for a in range(G):
                copy_xt(NG - G + a)
                nc.scalar.activation(mask_sb[:, 0, a, :], adj_sb[:, 0, a, :].bitcast(i32), ACT.Relu,
                                     scale=MASK_SCALE).then_inc(mask_ready, 1)

            def mask(g, c, first):
                act.wait_ge(adj_in[c % AR], g * (16 * NC // AR) + 16 * (c // AR + 1))
                if not (first and c < MR):
                    act.wait_ge(tr_ready, g * (NC * BC) + (c - MR + 1) * BC)
                nc.scalar.activation(mask_sb[:, c % MR, :, :], adj_sb[:, c % AR, :, :].bitcast(i32),
                                     ACT.Relu, scale=MASK_SCALE).then_inc(mask_ready, G)

            def std_of(g):
                act.wait_ge(var_ready, g + 1)
                nc.scalar.activation(std[:, :], mv[:, :, 1], ACT.Sqrt, bias=eps_sb[:, :]).then_inc(std_ready, 1)

            act.wait_ge(shift_ready, 1)
            act.wait_ge(st_ready, 1)
            nc.scalar.activation(v[:, :], st[:, 1, :], ACT.Exp, bias=shift2[:, :], scale=SLOPE).then_inc(v_ready, 1)
            nc.scalar.activation(rho_col[:, :], st[:, 0, :], ACT.Exp, bias=shift8[:, :],
                                 scale=-(1.0 - SLOPE)).then_inc(rhocol_exp, 1)
            nc.scalar.activation(q[:, :], st[:, 1, :], ACT.Exp, bias=shift8[:, :],
                                 scale=1.0 - SLOPE).then_inc(q_ready, 1)
            act.wait_ge(consts_ready, 1)
            for c in range(1, NC):
                mask(0, c, True)
            with act.Fori(1, NG) as g:
                for c in range(NC):
                    mask(g, c, False)
                    if c == 2:
                        std_of(g - 1)
            std_of(NG - 1)

        @block.vector
        def _(dve):
            nc.vector.memset(eps_sb[:, :], EPS).then_inc(consts_ready, 1)
            dve.wait_ge(wt_psum, 1)
            nc.vector.tensor_copy(wt[:, :], rho_ps[:, 0:D]).then_inc(wt_ready, 1)
            dve.wait_ge(w_in, 16)
            dve.wait_ge(wa_psum, 1)
            nc.vector.tensor_copy(w_ext[:, D:D + 2], acc[0][:, 0:2]).then_inc(wext_ready, 1)
            with dve.Fori(0, NG) as g:
                for a in range(G):
                    dve.wait_ge(wh_psum, g * G + (a + 1))
                    nc.vector.tensor_copy(whv[:, bass.ds(g * G + a, 1), :].rearrange("p t d -> p (t d)"),
                                          acc[a][:, 0:D + 2]).then_inc(acc_taken, 1)
            dve.wait_ge(acc_taken, RT)
            nc.vector.reduce_max(tmax_p[:, :], whv[:, :, D + 1], AX.X).then_inc(tmaxp_ready, 1)
            nc.vector.tensor_copy(st[:, :, :], whv[:, :, D:D + 2].rearrange("p t k -> p k t")).then_inc(st_ready, 1)
            dve.wait_ge(st_ready, 1)
            nc.vector.memset(whv[:, :, D:D + 1], 1.0).then_inc(ones_ready, 1)
            dve.wait_ge(tmax_ready, 1)
            nc.vector.tensor_scalar(shift8[:, :], tmax[:, :], -(1.0 - SLOPE), None, ALU.mult)
            nc.vector.tensor_scalar(shift2[:, :], tmax[:, :], -SLOPE, None, ALU.mult).then_inc(shift_ready, 1)
            dve.wait_ge(rhocol_exp, 1)
            nc.vector.tensor_scalar(rho_col[:, :], rho_col[:, :], 1.0, None, ALU.min).then_inc(rhocol_ready, 1)
            dve.wait_ge(q_ready, 1)

            def copy_rho(g):
                dve.wait_ge(rho_psum, g + 1)
                if not isinstance(g, int) or g > 0:
                    dve.wait_ge(pt_ready, g * RT)
                nc.vector.tensor_copy(rho[:, :], rho_ps[:, :]).then_inc(rho_ready, 1)

            def stage_rho(g):
                nc.vector.tensor_copy(rho_next[:, :], rho_col[:, bass.ds(g * G, G)]).then_inc(rho_next_ready, 1)

            def self_loops():
                dve.wait_ge(rhocol_ready, 1)
                nc.vector.tensor_tensor(top[:, :], rho_col[:, :], q[:, :], ALU.max).then_inc(self_step, 1)
                dve.wait_ge(self_step, 1)
                dve.wait_ge(diag_in, 16 * G)
                nc.vector.scalar_tensor_tensor(out=self_num[:, :], in0=diag.rearrange("p g a o -> p (g a o)"),
                                               scalar=0.0, in1=top[:, :],
                                               op0=ALU.is_le, op1=ALU.mult).then_inc(self_step, 1)

            def numerators(g, p, k, first):
                n = g * RT + p * PAIR + k
                if k == 0:
                    dve.wait_ge(rho_ready, g + 1)
                if k % PK == 0:
                    dve.wait_ge(tr_ready, g * (NC * BC) + p * (2 * BC) + (k // PK + 1))
                if not (first and k < PR):
                    dve.wait_ge(pt_used, n - (PR - 1))
                nc.vector.scalar_tensor_tensor(
                    out=pt[:, k % PR, :], in0=rho[:, :], scalar=q[:, bass.ds(p * PAIR + k, 1)],
                    in1=tr_mask[k // PK % TR][k % PK], op0=ALU.max, op1=ALU.min).then_inc(pt_ready, 1)

            def take_sums(g):
                for a in range(G):
                    dve.wait_ge(acc_ready, g * G + (a + 1))
                    nc.vector.scalar_tensor_tensor(
                        out=num[:, a, :], in0=whv[:, bass.ds(g * G + a, 1), 0:DE].rearrange("p t d -> p (t d)"),
                        scalar=self_num[:, bass.ds(g * G + a, 1)], in1=acc[a][:, 0:DE],
                        op0=ALU.mult, op1=ALU.add).then_inc(acc_taken, 1)

            def invert_denominators(g):
                dve.wait_ge(acc_taken, g * G + (RT + G))
                nc.vector.reciprocal(rden[:, :], num[:, :, D]).then_inc(rden_ready, 1)

            def add_residual(g):
                dve.wait_ge(rden_ready, g + 1)
                for a in range(G):
                    nc.vector.scalar_tensor_tensor(out=y[:, a, :], in0=num[:, a, 0:D], scalar=rden[:, a:a + 1],
                                                   in1=x_sb[:, bass.ds(g, 1), a, :].rearrange("p g d -> p (g d)"),
                                                   op0=ALU.mult, op1=ALU.add).then_inc(y_ready, 1)

            def row_stats(g):
                for a in range(G):
                    dve.wait_ge(y_ready, g * G + (a + 1))
                    last = nc.vector.bn_stats(stats[:, a, :], y[:, a, :])
                last.then_inc(stats_ready, 1)

            def row_variances():
                for a in range(G):
                    last = nc.vector.bn_aggr(mv[:, a, :], stats[:, a, :])
                last.then_inc(var_ready, 1)

            def invert_std(g):
                dve.wait_ge(std_ready, g + 1)
                nc.vector.reciprocal(rstd[:, :], std[:, :]).then_inc(rstd_ready, 1)

            def normalise(g):
                dve.wait_ge(rstd_ready, g + 1)
                dve.wait_ge(var_ready, g + 1)
                if not isinstance(g, int) or g > 0:
                    dve.wait_ge(o_out, g * 16)
                for a in range(G):
                    last = nc.vector.tensor_scalar(o_sb[:, a, :], y[:, a, :], mv[:, a, 0:1], rstd[:, a:a + 1],
                                                   ALU.subtract, ALU.mult)
                last.then_inc(o_ready, 1)

            def pair(g, p, first):
                for k in range(PAIR):
                    numerators(g, p, k, first)

            dve.wait_ge(rhocol_ready, 1)
            stage_rho(0)
            copy_rho(0)
            dve.wait_ge(rho_ready, 1)
            stage_rho(1)
            pair(0, 0, True)
            self_loops()
            with dve.Fori(1, NP) as p:
                pair(0, p, False)
            dve.wait_ge(self_step, 2)

            def group(g, last):
                copy_rho(g)
                for k in range(PAIR):
                    if k == 8:
                        dve.wait_ge(stats_ready, g)
                    numerators(g, 0, k, False)
                    if k == 0 and not last:
                        stage_rho(g + 1)
                    elif k == 2:
                        take_sums(g - 1)
                    elif k == 3:
                        invert_denominators(g - 1)
                    elif k == 4:
                        add_residual(g - 1)
                    elif k == 6:
                        row_stats(g - 1)
                    elif k == 8:
                        row_variances()
                    elif k == PAIR - 2:
                        invert_std(g - 1)
                    elif k == PAIR - 1:
                        normalise(g - 1)
                with dve.Fori(1, NP) as p:
                    pair(g, p, False)

            with dve.Fori(1, NG - 1) as g:
                group(g, False)
            group(NG - 1, True)
            take_sums(NG - 1)
            invert_denominators(NG - 1)
            add_residual(NG - 1)
            row_stats(NG - 1)
            dve.wait_ge(stats_ready, NG)
            row_variances()
            invert_std(NG - 1)
            normalise(NG - 1)

        @block.tensor
        def _(pe):
            pe.wait_ge(ident_ready, 1)
            pe.wait_ge(w_in, 16)
            nc.tensor.transpose(rho_ps[:, 0:D], w_ext[:, 0:D], ident[:, :]).then_inc(wt_psum, 1)

            def transpose_x(g):
                if g in X_PIECES:
                    pe.wait_ge(x_in[X_PIECES.index(g)], 16)
                if g >= TR:
                    pe.wait_ge(xt_ready, g - TR + 1)
                for a in range(G):
                    last = nc.tensor.transpose(tr[g % TR][:, a * P:(a + 1) * P], x_sb[:, g, a, :], ident[:, :])
                last.then_inc(xt_psum, 1)

            def project_x(g):
                pe.wait_ge(xt_ready, g + 1)
                for a in range(G):
                    if g > 0:
                        pe.wait_ge(acc_taken, (g - 1) * G + a + 1)
                    nc.tensor.matmul(acc[a][:, 0:D + 2], xt[:, g % XT, a * P:(a + 1) * P], w_ext[:, :],
                                     start=True, stop=True).then_inc(wh_psum, 1)

            transpose_x(0)
            pe.wait_ge(wt_ready, 1)
            pe.wait_ge(a_in, 16)
            nc.tensor.matmul(acc[0][:, 0:2], wt[:, :], a_sb[:, :], start=True, stop=True).then_inc(wa_psum, 1)
            pe.wait_ge(wext_ready, 1)
            for g in range(NG):
                if g + 1 < NG:
                    transpose_x(g + 1)
                project_x(g)

            def spread_rho(g):
                pe.wait_ge(rho_next_ready, g + 1)
                for a in range(G):
                    last = nc.tensor.transpose(rho_ps[:, a * P:(a + 1) * P],
                                               rho_next[:, a:a + 1].broadcast_to([P, P]), ident[:, :])
                last.then_inc(rho_psum, 1)

            def transpose_mask(g, p, m):
                if m % BC == 0:
                    pe.wait_ge(mask_ready, g * (NC * G) + p * (2 * G) + (m // BC + 1) * G)
                words = mask_sb[:, m // BC % MR, :, :].bitcast(fp32).rearrange(
                    "p a (c w r) -> p a c r w", w=P, r=G // PK)[:, :, m % BC // (G // PK), m % (G // PK), :]
                for a in range(G):
                    last = nc.tensor.transpose(tr[m % TR][:, a * P:(a + 1) * P], words[:, a, :], ident[:, :])
                last.then_inc(tr_ready, 1)

            def pair(g, p, first, last, final, spread=False, scaled=False):
                for k in range(PAIR):
                    if scaled and k % VC == 0:
                        pe.wait_ge(whv_ready, p * (PAIR // VC) + (k // VC + 1))
                    if spread and k == RHO_AT:
                        spread_rho(g + 1)
                    n = g * RT + p * PAIR + k
                    m = k // PK + LEAD
                    if k % PK == 0 and (m < 2 * BC or not final):
                        transpose_mask(g, p, m)
                    pe.wait_ge(pt_ready, n + 1)
                    for a in range(G):
                        if first and k == 0:
                            pe.wait_ge(acc_taken, (g - 1) * G + (RT + a + 1))
                        mm = nc.tensor.matmul(
                            acc[a][:, 0:DE], pt[:, k % PR, a * P:(a + 1) * P],
                            whv[:, bass.ds(p * PAIR + k, 1), 0:DE].rearrange("p t d -> p (t d)"),
                            start=first and k == 0, stop=last and k == PAIR - 1)
                        if last and k == PAIR - 1:
                            mm.then_inc(acc_ready, 1)
                        elif a == G - 1:
                            mm.then_inc(pt_used, 1)
                    if last and k == PAIR - 1:
                        pe.wait_ge(acc_ready, (g + 1) * G)
                        pe.sem_inc(pt_used, 1)

            pe.wait_ge(xt_ready, NG)
            for m in range(LEAD):
                transpose_mask(0, 0, m)
            spread_rho(0)

            def group(g, spread, scaled=False, final=False):
                pair(g, 0, True, False, False, spread, scaled)
                with pe.Fori(1, NP - 1) as p:
                    pair(g, p, False, False, False, False, scaled)
                pair(g, NP - 1, False, True, final, False, scaled)

            group(0, True, scaled=True)
            with pe.Fori(1, NG - 1) as g:
                group(g, True)
            group(NG - 1, False, final=True)


_INS = ["x", "adj", "L0_gnn_W", "L0_gnn_a"]
_OUTS = [((8192, 128), "float32")]


def kernel(**inputs):
    import numpy as _np
    import concourse.bacc as _bacc
    from concourse import mybir as _mybir
    from concourse.bass_utils import run_bass_kernel_spmd as _run

    nc = _bacc.Bacc("TRN2", target_bir_lowering=False, num_devices=1)
    arrays, args = {}, []
    for name in _INS:
        a = _np.ascontiguousarray(inputs[name])
        arrays[f"in_{name}_dram"] = a
        args.append(nc.dram_tensor(f"in_{name}_dram", a.shape, _mybir.dt.from_np(a.dtype), kind="ExternalInput").ap())
    for i, (shape, dtype) in enumerate(_OUTS):
        dt = _mybir.dt.from_np(_np.dtype(dtype))
        args.append(nc.dram_tensor(f"out_{i}_dram", shape, dt, kind="ExternalOutput").ap())
    gat_resnorm_kernel(nc, *args)
    r = _run(nc, [arrays], core_ids=[0])
    return r.results[0]["out_0_dram"]
```

```python
import concourse.bass as bass
from concourse import mybir
from contextlib import ExitStack


def gat_resnorm_kernel(nc: bass.Bass, x_dram: bass.AP, adj_dram: bass.AP, w_dram: bass.AP, a_dram: bass.AP,
                       out_dram: bass.AP):
    fp32 = mybir.dt.float32
    i32 = mybir.dt.int32
    u32 = mybir.dt.uint32
    u8 = mybir.dt.uint8
    ALU = mybir.AluOpType
    ACT = mybir.ActivationFunctionType
    AX = mybir.AxisListType

    P = 128
    N, D = x_dram.shape
    SLOPE = 0.2
    EPS = 1e-5
    RT = N // P
    G = 4
    Q = 4
    S = P // Q
    GR = G * P
    NG = RT // G
    H = 2
    CH = Q * G * H * S
    CQ = CH // Q
    CT = CH // P
    NC = N // CH
    PAIR = 2 * CT
    NP = NC // 2
    AR = 4
    WORDS = GR
    WG = NC * H
    MR = 4
    MT = 2
    TR = 2
    PR = 8
    XT = 4
    WB = 2
    FIRST = RT // WB
    NS = NG // H
    DE = D + 1
    VC = 4
    RANGE = 40.0
    TINY = 1e-30
    LOW = -1e30
    MASK_SCALE = 2.0 ** -23

    nodes = dict(b=Q, a=G, h=H, r=S)
    x_rows = x_dram.rearrange("(n b u r) d -> r n b u d", b=Q, u=G * H, r=S)
    out_rows = out_dram.rearrange("(n b a h r) d -> r n b h a d", **nodes)
    adj_rows = adj_dram.rearrange("(n b a h r) j -> r n h (b a) j", **nodes)
    adj_tile_rows = adj_dram.rearrange("(n b a h r) j -> r n b h a j", **nodes)

    def quadrant(b):
        return slice(b * S, (b + 1) * S)

    ctx = ExitStack()
    with ctx:
        def sb(name, shape, dt):
            return ctx.enter_context(nc.sbuf_tensor(name, shape, dt))

        def sem(name):
            return ctx.enter_context(nc.semaphore(name))

        adj_sb = sb("adj_sb", [P, AR, Q * G, CQ], fp32)
        mask_sb = sb("mask_sb", [P, MR, WORDS * G], u8)
        mask_t = sb("mask_t", [P, MT, WORDS], u32)
        rho = sb("rho", [P, N], fp32)
        whv = sb("whv", [P, RT, D + 2], fp32)
        pt = sb("pt", [P, PR, GR], fp32)
        x_sb = sb("x_sb", [P, NS, G * H, D], fp32)
        xt = pt[:, PR - XT:PR, :]
        w_ext = sb("w_ext", [P, D + 2], fp32)
        wt = sb("wt", [P, D], fp32)
        a_sb = sb("a_sb", [P, 2], fp32)
        ident = sb("ident", [P, P], fp32)
        st = sb("st", [P, 2, RT], fp32)
        tmax_p = sb("tmax_p", [P, 1], fp32)
        tneg_p = sb("tneg_p", [P, 1], fp32)
        tneg = sb("tneg", [P, 1], fp32)
        wide = sb("wide", [P, 1], i32)
        above = sb("above", [P, RT], fp32)
        den = sb("den", [P, G], fp32)
        tmax = sb("tmax", [P, 1], fp32)
        shift8 = sb("shift8", [P, 1], fp32)
        shift2 = sb("shift2", [P, 1], fp32)
        q = sb("q", [P, RT], fp32)
        v = sb("v", [P, RT], fp32)
        rho_col = sb("rho_col", [P, P], fp32)
        rho_rows = sb("rho_rows", [RT, P], fp32)
        diag = sb("diag", [P, RT], fp32)
        top = sb("top", [P, RT], fp32)
        self_num = sb("self_num", [P, RT], fp32)
        num = sb("num", [P, G, DE], fp32)
        rden = sb("rden", [P, G], fp32)
        y = sb("y", [P, G, D], fp32)
        stats = sb("stats", [P, G, 6], fp32)
        mv = sb("mv", [P, G, 2], fp32)
        eps_sb = sb("eps_sb", [P, 1], fp32)
        std = sb("std", [P, G], fp32)
        rstd = sb("rstd", [P, G], fp32)
        shift = sb("shift", [P, G], fp32)
        o_sb = sb("o_sb", [P, G, D], fp32)
        e_row = adj_sb[:, 0:2, :, :].rearrange("p s m c -> p (s m c)")
        t_row = adj_sb[:, 2:4, :, :].rearrange("p s m c -> p (s m c)")
        w_x = rho.rearrange("p (k d) -> p k d", d=D)
        t_next = sb("t_next", [P, G], fp32)
        w_t = sb("w_t", [P, 2], fp32)
        w_self = sb("w_self", [P, 2], fp32)
        w_max = sb("w_max", [P, 3], fp32)
        w_exp = sb("w_exp", [P, 1], fp32)
        w_add = sb("w_add", [P, 1], fp32)
        w_den = sb("w_den", [P, 3], fp32)
        w_px = sb("w_px", [P, D], fp32)
        w_pxt = sb("w_pxt", [P, D], fp32)
        w_y = sb("w_y", [P, D], fp32)
        w_o = sb("w_o", [P, D], fp32)
        w_mean = sb("w_mean", [P, 2], fp32)
        w_sq = sb("w_sq", [P, D], fp32)
        w_var = sb("w_var", [P, 1], fp32)
        w_std = sb("w_std", [P, 2], fp32)

        acc = [[ctx.enter_context(nc.psum_tensor(f"acc{h}{a}", [P, 512], fp32)) for a in range(G)] for h in range(H)]
        tr, rho_ps, rho_t_ps = acc[1][0:TR], acc[1][TR], acc[1][TR + 1]
        rho_dram = nc.dram_tensor("rho_dram", (RT, P), fp32, kind="Internal").ap()
        acc_wh = [t[:, :].rearrange("p (w c) -> p w c", w=WB)[:, :, 0:D + 2] for t in acc[0]]
        mask_bytes = [mask_t[:, k, :].bitcast(u8).rearrange("p (i a) -> p i a", a=G) for k in range(MT)]
        x_in = [sem(f"x_in{n}") for n in range(NS)]
        x_last_in = [sem(f"x_last_in{n}") for n in range(NS)]
        w_in = sem("w_in")
        a_in = sem("a_in")
        diag_in = sem("diag_in")
        adj_in = [sem(f"adj_in{k}") for k in range(AR)]
        zeroed = sem("zeroed")
        ident_ready = sem("ident_ready")
        consts_ready = sem("consts_ready")
        wt_psum = sem("wt_psum")
        wt_ready = sem("wt_ready")
        wa_psum = sem("wa_psum")
        wext_ready = sem("wext_ready")
        xt_psum = sem("xt_psum")
        xt_ready = sem("xt_ready")
        wh_psum = sem("wh_psum")
        st_ready = sem("st_ready")
        tmaxp_ready = sem("tmaxp_ready")
        tmax_ready = sem("tmax_ready")
        shift_ready = sem("shift_ready")
        v_ready = sem("v_ready")
        q_ready = sem("q_ready")
        above_ready = sem("above_ready")
        rhocol_ready = sem("rhocol_ready")
        tneg_step = sem("tneg_step")
        tnegp_ready = sem("tnegp_ready")
        tneg_ready = sem("tneg_ready")
        wide_ready = sem("wide_ready")
        self_step = sem("self_step")
        ones_ready = sem("ones_ready")
        whv_ready = sem("whv_ready")
        rho_psum = sem("rho_psum")
        rho_ready = sem("rho_ready")
        rho_t_psum = sem("rho_t_psum")
        rho_rows_ready = sem("rho_rows_ready")
        rho_out = sem("rho_out")
        rho_in = sem("rho_in")
        mask_ready = sem("mask_ready")
        mask_t_ready = sem("mask_t_ready")
        pt_ready = sem("pt_ready")
        pt_used = sem("pt_used")
        acc_ready = sem("acc_ready")
        acc_taken = sem("acc_taken")
        den_ready = sem("den_ready")
        rden_ready = sem("rden_ready")
        mean_ready = sem("mean_ready")
        y_ready = sem("y_ready")
        stats_ready = sem("stats_ready")
        var_ready = sem("var_ready")
        std_ready = sem("std_ready")
        inv_ready = sem("inv_ready")
        rstd_ready = sem("rstd_ready")
        o_ready = sem("o_ready")
        o_rest_ready = sem("o_rest_ready")
        o_out = sem("o_out")
        w_tnext_ready = sem("w_tnext_ready")
        w_spread = sem("w_spread")
        w_trow_ready = sem("w_trow_ready")
        w_free = sem("w_free")
        w_x_in = sem("w_x_in")
        w_in_adj = sem("w_in_adj")
        w_own = sem("w_own")
        w_scores = sem("w_scores")
        w_nums = sem("w_nums")
        w_tr = sem("w_tr")
        w_copied = sem("w_copied")
        w_mult = sem("w_mult")
        w_px_ready = sem("w_px_ready")
        w_pxt_psum = sem("w_pxt_psum")
        w_pxt_ready = sem("w_pxt_ready")
        w_h = sem("w_h")
        w_var_ready = sem("w_var_ready")
        w_std_ready = sem("w_std_ready")
        w_o_ready = sem("w_o_ready")
        w_out = sem("w_out")

        def load_adj(queue, n, h, c):
            for b in (range(Q // 2) if queue is nc.sync else range(Q // 2, Q)):
                queue.dma_start(adj_sb[quadrant(b), c % AR, :, :],
                                adj_rows[:, bass.ds(n, 1), h, :, c % NC * CH + b * CQ:c % NC * CH + (b + 1) * CQ]
                                ).then_inc(adj_in[c % AR], 16)

        block = ctx.enter_context(nc.Block())

        @block.sync
        def _(sp):
            def spread_rho(n, h):
                sp.dma_start(rho[:, bass.ds((n * H + h) * GR, GR)],
                             rho_dram[bass.ds((n * H + h) * G, G), :].rearrange("a i -> (a i)").unsqueeze(0)
                             .broadcast_to([P, GR])).then_inc(rho_in, 16)

            def store(n, h):
                sp.wait_ge(o_ready, n * H + (h + 1))
                for b in range(Q):
                    sp.dma_start(out_rows[:, bass.ds(n, 1), b, h, :, :], o_sb[quadrant(b), :, :]).then_inc(o_out, 16)

            def group(n, h):
                spread_rho(n, h)
                for c in range(NC):
                    sp.wait_ge(mask_ready, n * (H * WG) + (h * WG + (c - AR + 1) * H))
                    load_adj(nc.sync, n, h, c)

            for n in range(NS):
                for b in range(Q - 1):
                    sp.dma_start(x_sb[quadrant(b), n, :, :], x_rows[:, n, b, :, :]).then_inc(x_in[n], 16)
            for c in range(NC):
                if c == AR:
                    sp.wait_ge(rho_rows_ready, 1)
                    sp.dma_start(rho_dram, rho_rows[:, :]).then_inc(rho_out, 16)
                if c >= AR:
                    sp.wait_ge(mask_ready, (c - AR + 1) * H)
                load_adj(nc.sync, 0, 0, c)
            sp.wait_ge(rho_out, 16)
            for h in range(1, H):
                group(0, h)
                store(0, h - 1)
            with sp.Fori(1, NS) as n:
                for h in range(H):
                    group(n, h)
                    if h == 0:
                        store(n - 1, H - 1)
                    else:
                        store(n, h - 1)
            sp.wait_ge(o_rest_ready, 1)
            store(NS - 1, H - 1)
            sp.wait_ge(o_out, 16 * Q * NG)

            sp.wait_ge(wide_ready, 1)
            is_wide = sp.value_load(wide[0:1, 0:1], min_val=0, max_val=1)
            with sp.If(is_wide > 0):
                sp.dma_start(w_x, x_dram.rearrange("(k p) d -> p k d", p=P)).then_inc(w_x_in, 16)
                with sp.Fori(0, NS) as n:
                    for k in range(H * G):
                        h, a = k // G, k % G
                        sp.wait_ge(w_free, n * (H * G) + (k + 1))
                        for b in range(Q):
                            sp.dma_start(e_row[quadrant(b), :],
                                         adj_tile_rows[:, bass.ds(n, 1), b, h, a, :]).then_inc(w_in_adj, 16)
                        sp.wait_ge(w_o_ready, n * (H * G) + (k + 1))
                        for b in range(Q):
                            sp.dma_start(out_rows[:, bass.ds(n, 1), b, h, a, :],
                                         w_o[quadrant(b), :]).then_inc(w_out, 16)
                sp.wait_ge(w_out, 16 * Q * RT)

        @block.gpsimd
        def _(pool):
            def load_x(n):
                pool.dma_start(x_sb[quadrant(Q - 1), n, :, :], x_rows[:, n, Q - 1, :, :]).then_inc(x_last_in[n], 16)

            load_x(0)
            nc.gpsimd.memset(ident[:, :], 0.0).then_inc(zeroed, 1)
            pool.wait_ge(zeroed, 1)
            nc.gpsimd.affine_select(out=ident[:, :], in_=ident[:, :], compare_op=ALU.not_equal, fill=1.0, base=0,
                                    pattern=[[-1, P]], channel_multiplier=1).then_inc(ident_ready, 1)
            for n in range(1, NS):
                load_x(n)

            def load_diagonal(pieces):
                with nc.allow_non_contiguous_dma(reason="the diagonal of adj"):
                    for k in pieces:
                        b, h, a = k // (H * G), k // G % H, k % G
                        pool.dma_start(diag[quadrant(b), h * G + a:RT:H * G],
                                       bass.AP(tensor=adj_dram.tensor, offset=(((b * G + a) * H + h) * S) * (N + 1),
                                               ap=[[N + 1, S], [CH * (N + 1), NS], [1, 1]])).then_inc(diag_in, 16)

            early = 12
            load_diagonal(range(early))
            pool.wait_ge(tmaxp_ready, 1)
            nc.gpsimd.partition_all_reduce(tmax[:, :], tmax_p[:, :], P,
                                           bass.bass_isa.ReduceOp.max).then_inc(tmax_ready, 1)
            pool.wait_ge(acc_taken, FIRST)
            pool.wait_ge(ones_ready, 1)
            pool.wait_ge(v_ready, 1)
            for k in range(0, RT, VC):
                piece = whv[:, k:k + VC, 0:DE]
                nc.gpsimd.tensor_tensor(piece, piece, v[:, k:k + VC].unsqueeze(2).broadcast_to([P, VC, DE]),
                                        ALU.mult).then_inc(whv_ready, 1)
            pool.wait_ge(tnegp_ready, 1)
            nc.gpsimd.partition_all_reduce(tneg[:, :], tneg_p[:, :], P,
                                           bass.bass_isa.ReduceOp.max).then_inc(tneg_ready, 1)
            load_diagonal(range(early, Q * H * G))

            def add_residual(g, n, h):
                pool.wait_ge(rden_ready, g + 1)
                if not isinstance(g, int) or g > 0:
                    pool.wait_ge(o_ready, g)
                nc.gpsimd.tensor_tensor(y[:, :, :], num[:, :, 0:D], rden[:, :].unsqueeze(2).broadcast_to([P, G, D]),
                                        ALU.mult).then_inc(mean_ready, 1)
                pool.wait_ge(mean_ready, g + 1)
                nc.gpsimd.tensor_tensor(y[:, :, :], y[:, :, :],
                                        x_sb[:, bass.ds(n, 1), h:G * H:H, :].rearrange("p n a d -> p (n a) d"),
                                        ALU.add).then_inc(y_ready, 1)

            add_residual(0, 0, 0)
            with pool.Fori(1, NS) as n:
                add_residual(n * H - 1, n - 1, H - 1)
                for h in range(H - 1):
                    add_residual(n * H + h, n, h)

        @block.scalar
        def _(act):
            act.dma_start(w_ext[:, 0:D], w_dram).then_inc(w_in, 16)
            with nc.allow_non_contiguous_dma(reason="a_src and a_dst as columns"):
                act.dma_start(a_sb[:, :], a_dram.rearrange("(k p) -> p k", p=P)).then_inc(a_in, 16)

            def copy_xt(g):
                act.wait_ge(xt_psum, g + 1)
                if g >= XT:
                    act.wait_ge(wh_psum, (g - XT + 1) * (G // WB))
                nc.scalar.copy(xt[:, g % XT, :], tr[g % TR][:, :]).then_inc(xt_ready, 1)

            for g in range(NG - G):
                copy_xt(g)
                if g == G:
                    load_adj(nc.scalar, 0, 0, 0)
                elif g == 2 * G:
                    load_adj(nc.scalar, 0, 0, 1)

            def mask(slot, w, rows=slice(0, Q * G)):
                bits = adj_sb[:, slot, :, :].bitcast(i32).rearrange("p m (a h r) -> p h m r a", a=G, h=H)[:, w]
                words = mask_sb[:, (slot * H + w) % MR, :].rearrange("p (m r a) -> p m r a", r=S, a=G)
                return nc.scalar.activation(words[:, rows, :, :], bits[:, rows, :, :], ACT.Relu, scale=MASK_SCALE)

            act.wait_ge(adj_in[0], 16 * Q)
            for k in range(G):
                copy_xt(NG - G + k)
                half = Q * G // 2
                last = mask(0, k // 2, slice(k % 2 * half, k % 2 * half + half))
                if k % 2 == 1:
                    last.then_inc(mask_ready, 1)

            def mask_chunk(n, h, c, last):
                g = n * H + h
                first = isinstance(g, int) and g == 0
                act.wait_ge(adj_in[c % AR], g * (16 * Q * NC // AR) + 16 * Q * (c // AR + 1))
                for w in range(H):
                    if not (first and c * H + w < MR):
                        act.wait_ge(mask_t_ready, g * WG + (c * H + w - MR + 1))
                    if w == H - 1:
                        act.wait_ge(mask_ready, g * WG + c * H)
                    mask(c % AR, w).then_inc(mask_ready, 1)
                c = c - 1 + AR
                if c < NC:
                    load_adj(nc.scalar, n, h, c)
                elif not last:
                    load_adj(nc.scalar, *((n, h + 1) if h < H - 1 else (n + 1, 0)), c)

            def std_of(g):
                act.wait_ge(var_ready, g + 1)
                nc.scalar.activation(std[:, :], mv[:, :, 1], ACT.Sqrt, bias=eps_sb[:, :]).then_inc(std_ready, 1)

            def normalise(g, tiles=range(G)):
                act.wait_ge(rstd_ready, g + 1)
                if not isinstance(g, int) or g > 0:
                    act.wait_ge(o_out, g * (16 * Q))
                for a in tiles:
                    last = nc.scalar.activation(o_sb[:, a, :], y[:, a, :], ACT.Identity, bias=shift[:, a:a + 1],
                                                scale=rstd[:, a:a + 1])
                last.then_inc(o_ready, 1)

            act.wait_ge(shift_ready, 1)
            act.wait_ge(st_ready, 1)
            act.wait_ge(above_ready, 1)
            nc.scalar.activation(rho_col[:, 0:RT], above[:, :], ACT.Exp, scale=-(1.0 - SLOPE)).then_inc(rhocol_ready, 1)
            nc.scalar.activation(v[:, :], st[:, 1, :], ACT.Exp, bias=shift2[:, :], scale=SLOPE).then_inc(v_ready, 1)
            nc.scalar.activation(q[:, :], st[:, 1, :], ACT.Exp, bias=shift8[:, :],
                                 scale=1.0 - SLOPE).then_inc(q_ready, 1)
            for c in range(2, AR):
                load_adj(nc.scalar, 0, 0, c)
            act.wait_ge(consts_ready, 1)
            for c in range(1, NC):
                mask_chunk(0, 0, c, False)

            def group(n, h, last=False):
                g = n * H + h
                for c in range(NC):
                    mask_chunk(n, h, c, last)
                    if c == 3:
                        std_of(g - 1)
                    elif c == 4:
                        normalise(g - 1)

            for h in range(1, H):
                group(0, h)
            with act.Fori(1, NS - 1) as n:
                for h in range(H):
                    group(n, h)
            for h in range(H):
                group(NS - 1, h, h == H - 1)
            std_of(NG - 1)
            normalise(NG - 1, range(G // 2))

            act.wait_ge(wide_ready, 1)
            is_wide = act.value_load(wide[0:1, 0:1], min_val=0, max_val=1)
            with act.If(is_wide > 0):
                with act.Fori(0, RT) as r:
                    act.wait_ge(w_scores, r + 1)
                    nc.scalar.activation(e_row, e_row, ACT.Exp, bias=w_max[:, 2:3], accum_out=w_den[:, 0:1])
                    nc.scalar.activation(w_exp[:, :], w_self[:, 1:2], ACT.Exp, bias=w_max[:, 2:3]).then_inc(w_nums, 1)
                    for k in range(RT):
                        act.wait_ge(w_tr, r * RT + (k + 1))
                        if k >= PR:
                            act.wait_ge(w_mult, r * RT + (k - PR + 1))
                        nc.scalar.copy(pt[:, k % PR, 0:P], tr[k % TR][:, 0:P]).then_inc(w_copied, 1)
                    act.wait_ge(w_pxt_psum, r + 1)
                    nc.scalar.copy(w_pxt[:, :], tr[0][:, 0:P]).then_inc(w_pxt_ready, 1)
                    act.wait_ge(w_var_ready, r + 1)
                    nc.scalar.activation(w_std[:, 0:1], w_var[:, :], ACT.Sqrt, scale=1.0 / D,
                                         bias=eps_sb[:, :]).then_inc(w_std_ready, 1)

        @block.vector
        def _(dve):
            def transpose_mask(g, p, w, first):
                dve.wait_ge(mask_ready, g * WG + p * (2 * H) + (w + 1))
                if not (first and w < MT):
                    dve.wait_ge(pt_ready, g * RT + p * PAIR + (w - MT + 1) * G)
                nc.vector.transpose(mask_t[:, w % MT, :].rearrange("p (a b i) -> p b a i", a=G, b=Q),
                                    mask_sb[:, w % MR, :].bitcast(u32).rearrange("p (b a r) -> p b a r", a=G, b=Q)
                                    ).then_inc(mask_t_ready, 1)

            nc.vector.memset(rho_col[:, RT:P], 0.0)
            nc.vector.memset(eps_sb[:, :], EPS).then_inc(consts_ready, 1)
            dve.wait_ge(wt_psum, 1)
            nc.vector.tensor_copy(wt[:, :], rho_ps[:, 0:D]).then_inc(wt_ready, 1)
            dve.wait_ge(w_in, 16)
            dve.wait_ge(wa_psum, 1)
            nc.vector.tensor_copy(w_ext[:, D:D + 2], acc[0][0][:, 0:2]).then_inc(wext_ready, 1)
            with dve.Fori(0, FIRST // G) as b:
                for k in range(G):
                    dve.wait_ge(wh_psum, b * G + (k + 1))
                    nc.vector.tensor_copy(whv[:, bass.ds(b * (G * WB) + k * WB, WB), :],
                                          acc_wh[k]).then_inc(acc_taken, 1)
            dve.wait_ge(acc_taken, FIRST)
            nc.vector.reduce_max(tmax_p[:, :], whv[:, :, D + 1], AX.X).then_inc(tmaxp_ready, 1)
            nc.vector.tensor_copy(st[:, :, :], whv[:, :, D:D + 2].rearrange("p t k -> p k t")).then_inc(st_ready, 1)
            dve.wait_ge(st_ready, 1)
            nc.vector.memset(whv[:, :, D:D + 1], 1.0).then_inc(ones_ready, 1)
            dve.wait_ge(tmax_ready, 1)
            nc.vector.tensor_scalar(shift8[:, :], tmax[:, :], -(1.0 - SLOPE), None, ALU.mult)
            nc.vector.tensor_scalar(shift2[:, :], tmax[:, :], -SLOPE, None, ALU.mult).then_inc(shift_ready, 1)
            nc.vector.tensor_scalar(above[:, :], st[:, 0, :], tmax[:, :], 0.0,
                                    ALU.add, ALU.max).then_inc(above_ready, 1)
            transpose_mask(0, 0, 0, True)

            def self_loops():
                dve.wait_ge(rhocol_ready, 1)
                dve.wait_ge(diag_in, 16 * Q * H * G)
                nc.vector.tensor_tensor(top[:, :], rho_col[:, 0:RT], q[:, :], ALU.max).then_inc(self_step, 1)
                dve.wait_ge(self_step, 1)
                nc.vector.scalar_tensor_tensor(out=self_num[:, :], in0=diag[:, :],
                                               scalar=0.0, in1=top[:, :],
                                               op0=ALU.is_le, op1=ALU.mult).then_inc(self_step, 1)

            def span_of_t():
                nc.vector.tensor_reduce(tneg_p[:, :], st[:, 1, :], AX.X, ALU.min).then_inc(tneg_step, 1)
                dve.wait_ge(tneg_step, 1)
                nc.vector.tensor_scalar(tneg_p[:, :], tneg_p[:, :], -1.0, None, ALU.mult).then_inc(tnegp_ready, 1)

            def numerators(g, p, k, first, final=False):
                if k % G == 0:
                    dve.wait_ge(mask_t_ready, g * WG + p * (2 * H) + (k // G + 1))
                if k % G == 1 and not (final and k + G > PAIR):
                    transpose_mask(g, p, k // G + 1, first)
                if not isinstance(p, int) or p > 0 or k >= PR:
                    dve.wait_ge(pt_used, g * (RT - 1) + p * PAIR + (k - PR + 1))
                elif k == PR - 1 and not first:
                    dve.wait_ge(acc_ready, g * G)
                elif not first:
                    dve.wait_ge(pt_used, (g - 1) * (RT - 1) + (RT + k - PR + 1))
                from_psum = first and p == 0 and k == 0
                nc.vector.scalar_tensor_tensor(
                    out=pt[:, k % PR, :], in0=rho_ps[:, :] if from_psum else rho[:, bass.ds(g * GR, GR)],
                    scalar=q[:, bass.ds(p * PAIR + k, 1)], in1=mask_bytes[k // G % MT][:, :, k % G],
                    op0=ALU.max, op1=ALU.min).then_inc(pt_ready, 1)
                if from_psum:
                    nc.vector.tensor_copy(rho[:, 0:GR], rho_ps[:, :]).then_inc(rho_ready, 1)
                    dve.wait_ge(rho_ready, 1)

            def take_sums(g, h):
                for a in range(G):
                    dve.wait_ge(acc_ready, g * G + (a + 1))
                    nc.vector.scalar_tensor_tensor(
                        out=num[:, a, :], in0=whv[:, bass.ds(g * G + a, 1), 0:DE].rearrange("p t d -> p (t d)"),
                        scalar=self_num[:, bass.ds(g * G + a, 1)], in1=acc[h][a][:, 0:DE],
                        op0=ALU.mult, op1=ALU.add).then_inc(acc_taken, 1)

            def invert_denominators(g):
                dve.wait_ge(acc_taken, g * G + (FIRST + G))
                nc.vector.tensor_scalar(den[:, :], num[:, :, D], TINY, None, ALU.max).then_inc(den_ready, 1)
                dve.wait_ge(den_ready, g + 1)
                nc.vector.reciprocal(rden[:, :], den[:, :]).then_inc(rden_ready, 1)

            def row_stats(g):
                dve.wait_ge(y_ready, g + 1)
                for a in range(G):
                    last = nc.vector.bn_stats(stats[:, a, :], y[:, a, :])
                last.then_inc(stats_ready, 1)

            def row_variances():
                for a in range(G):
                    last = nc.vector.bn_aggr(mv[:, a, :], stats[:, a, :])
                last.then_inc(var_ready, 1)

            def invert_std(g):
                dve.wait_ge(std_ready, g + 1)
                nc.vector.reciprocal(rstd[:, :], std[:, :]).then_inc(inv_ready, 1)
                dve.wait_ge(inv_ready, g + 1)
                dve.wait_ge(var_ready, g + 1)
                nc.vector.scalar_tensor_tensor(out=shift[:, :], in0=mv[:, :, 0], scalar=-1.0, in1=rstd[:, :],
                                               op0=ALU.mult, op1=ALU.mult).then_inc(rstd_ready, 1)

            def pair(g, p, first, final=False):
                for k in range(PAIR):
                    numerators(g, p, k, first, final)

            dve.wait_ge(q_ready, 1)
            dve.wait_ge(rho_psum, 1)
            pair(0, 0, True)
            dve.wait_ge(rho_t_psum, 1)
            nc.vector.tensor_copy(rho_rows[:, :], rho_t_ps[0:RT, 0:P]).then_inc(rho_rows_ready, 1)
            span_of_t()
            with dve.Fori(1, NP) as p:
                pair(0, p, False)
            dve.wait_ge(tneg_ready, 1)
            nc.vector.tensor_scalar(wide[:, :], tneg[:, :], tmax[:, :], RANGE,
                                    ALU.add, ALU.is_ge).then_inc(wide_ready, 1)
            self_loops()
            dve.wait_ge(self_step, 2)

            def group(n, h, final=False):
                g = n * H + h
                before = (h - 1) % H
                dve.wait_ge(rho_in, g * 16)
                for k in range(PAIR):
                    if k == PR + 4:
                        dve.wait_ge(stats_ready, g)
                    numerators(g, 0, k, False)
                    if k == PR - 1:
                        take_sums(g - 1, before)
                    elif k == PR:
                        invert_denominators(g - 1)
                    elif k == PR + 3:
                        row_stats(g - 1)
                    elif k == PR + 4:
                        row_variances()
                    elif k == PAIR - 1:
                        invert_std(g - 1)
                with dve.Fori(1, NP - 1 if final else NP) as p:
                    pair(g, p, False)
                if final:
                    pair(g, NP - 1, False, True)

            for h in range(1, H):
                group(0, h)
            with dve.Fori(1, NS - 1) as n:
                for h in range(H):
                    group(n, h)
            for h in range(H):
                group(NS - 1, h, h == H - 1)

            take_sums(NG - 1, H - 1)
            invert_denominators(NG - 1)
            dve.wait_ge(rden_ready, NG)
            dve.wait_ge(o_ready, NG - 1)
            for a in range(G):
                last = nc.vector.scalar_tensor_tensor(out=y[:, a, :], in0=num[:, a, 0:D], scalar=rden[:, a:a + 1],
                                                      in1=x_sb[:, NS - 1, a * H + H - 1, :], op0=ALU.mult, op1=ALU.add)
            last.then_inc(y_ready, 1)
            row_stats(NG - 1)
            dve.wait_ge(stats_ready, NG)
            row_variances()
            invert_std(NG - 1)
            dve.wait_ge(inv_ready, NG)
            dve.wait_ge(o_out, (NG - 1) * (16 * Q))
            for a in range(G // 2, G):
                last = nc.vector.tensor_scalar(o_sb[:, a, :], y[:, a, :], mv[:, a, 0:1], rstd[:, a:a + 1],
                                               ALU.subtract, ALU.mult)
            last.then_inc(o_rest_ready, 1)

            def wide_tile(n, h, a):
                own = [0]

                def tied(instruction, least):
                    own[0] += 1
                    instruction.then_inc(w_own, 1)
                    dve.wait_ge(w_own, least + own[0])

                r = n * (H * G) + (h * G + a)
                s_i, t_i, adj_ii = st[:, 0, bass.ds(r, 1)], st[:, 1, bass.ds(r, 1)], diag[:, bass.ds(r, 1)]
                x_i = x_sb[:, bass.ds(n, 1), a * H + h, :].rearrange("p n d -> p (n d)")
                base = r * W_OWN
                dve.wait_ge(w_in_adj, r * (16 * Q) + 16 * Q)
                tied(nc.vector.tensor_scalar(e_row, e_row, 0.0, LOW, ALU.is_le, ALU.mult), base)
                tied(nc.vector.tensor_tensor(e_row, e_row, t_row, ALU.add), base)
                tied(nc.vector.reduce_max(w_t[:, 0:1], e_row, AX.X), base)
                tied(nc.vector.tensor_tensor(w_t[:, 1:2], w_t[:, 0:1], t_i, ALU.max), base)
                tied(nc.vector.tensor_tensor(w_max[:, 0:1], w_t[:, 1:2], s_i, ALU.add), base)
                tied(nc.vector.scalar_tensor_tensor(out=w_max[:, 1:2], in0=w_max[:, 0:1], scalar=SLOPE,
                                                    in1=w_max[:, 0:1], op0=ALU.mult, op1=ALU.max), base)
                tied(nc.vector.tensor_scalar(w_max[:, 2:3], w_max[:, 1:2], -1.0, None, ALU.mult), base)
                tied(nc.vector.tensor_tensor(w_self[:, 0:1], s_i, t_i, ALU.add), base)
                tied(nc.vector.scalar_tensor_tensor(out=w_self[:, 1:2], in0=w_self[:, 0:1], scalar=SLOPE,
                                                    in1=w_self[:, 0:1], op0=ALU.mult, op1=ALU.max), base)
                tied(nc.vector.tensor_scalar(e_row, e_row, s_i, None, ALU.add), base)
                nc.vector.scalar_tensor_tensor(out=e_row, in0=e_row, scalar=SLOPE, in1=e_row,
                                               op0=ALU.mult, op1=ALU.max).then_inc(w_scores, 1)
                dve.wait_ge(w_nums, r + 1)
                tied(nc.vector.scalar_tensor_tensor(out=w_add[:, :], in0=adj_ii, scalar=0.0, in1=w_exp[:, :],
                                                    op0=ALU.is_le, op1=ALU.mult), base)
                tied(nc.vector.tensor_tensor(w_den[:, 1:2], w_den[:, 0:1], w_add[:, :], ALU.add), base)
                tied(nc.vector.reciprocal(w_den[:, 2:3], w_den[:, 1:2]), base)
                dve.wait_ge(w_mult, r * RT + RT)
                nc.vector.scalar_tensor_tensor(out=w_px[:, :], in0=x_i, scalar=w_add[:, :], in1=acc[0][0][:, 0:D],
                                               op0=ALU.mult, op1=ALU.add).then_inc(w_px_ready, 1)
                dve.wait_ge(w_h, r + 1)
                tied(nc.vector.scalar_tensor_tensor(out=w_y[:, :], in0=acc[0][1][:, 0:D], scalar=w_den[:, 2:3], in1=x_i,
                                                    op0=ALU.mult, op1=ALU.add), base)
                tied(nc.vector.reduce_sum(w_mean[:, 0:1], w_y[:, :], AX.X), base)
                tied(nc.vector.tensor_scalar(w_mean[:, 1:2], w_mean[:, 0:1], 1.0 / D, None, ALU.mult), base)
                tied(nc.vector.tensor_scalar(w_y[:, :], w_y[:, :], w_mean[:, 1:2], None, ALU.subtract), base)
                tied(nc.vector.tensor_tensor(w_sq[:, :], w_y[:, :], w_y[:, :], ALU.mult), base)
                nc.vector.reduce_sum(w_var[:, :], w_sq[:, :], AX.X).then_inc(w_var_ready, 1)
                dve.wait_ge(w_std_ready, r + 1)
                tied(nc.vector.reciprocal(w_std[:, 1:2], w_std[:, 0:1]), base)
                nc.vector.tensor_scalar(w_o[:, :], w_y[:, :], w_std[:, 1:2], None, ALU.mult).then_inc(w_o_ready, 1)
                dve.wait_ge(w_out, r * (16 * Q) + 16 * Q)
                dve.sem_inc(w_free, 1)
                return own[0]

            W_OWN = 19
            t_row_tiles = t_row.rearrange("p (n b a h r) -> p n h a b r", **nodes)
            is_wide = dve.value_load(wide[0:1, 0:1], min_val=0, max_val=1)
            with dve.If(is_wide > 0):
                dve.wait_ge(o_out, 16 * Q * NG)
                with dve.Fori(0, NS) as n:
                    for h in range(H):
                        nc.vector.tensor_copy(t_next[:, :], st[:, 1, bass.ds(n * (H * G) + h * G, G)]
                                              ).then_inc(w_tnext_ready, 1)
                        dve.wait_ge(w_spread, n * H + (h + 1))
                        tiles = t_row_tiles[:, bass.ds(n, 1), h, :, :, :].rearrange("p n a b r -> p (n a) b r")
                        nc.vector.tensor_copy(tiles, rho_ps.rearrange("p (a b r) -> p a b r", a=G, b=Q)
                                              ).then_inc(w_trow_ready, 1)
                        dve.wait_ge(w_trow_ready, n * H + (h + 1))
                dve.sem_inc(w_free, 1)
                with dve.Fori(0, NS) as n:
                    for k in range(H * G):
                        assert wide_tile(n, k // G, k % G) == W_OWN

        @block.tensor
        def _(pe):
            pe.wait_ge(ident_ready, 1)
            pe.wait_ge(w_in, 16)
            nc.tensor.transpose(rho_ps[:, 0:D], w_ext[:, 0:D], ident[:, :]).then_inc(wt_psum, 1)

            def transpose_x(g):
                if g % H == 0:
                    pe.wait_ge(x_in[g // H], 16 * (Q - 1))
                    pe.wait_ge(x_last_in[g // H], 16)
                if g >= TR:
                    pe.wait_ge(xt_ready, g - TR + 1)
                for a in range(G):
                    last = nc.tensor.transpose(tr[g % TR][:, a * P:(a + 1) * P],
                                               x_sb[:, g // H, a * H + g % H, :], ident[:, :])
                last.then_inc(xt_psum, 1)

            def project_x(g):
                pe.wait_ge(xt_ready, g + 1)
                for a in range(G):
                    k = (g * G + a) // WB
                    if k >= G and a % WB == 0:
                        pe.wait_ge(acc_taken, k - G + 1)
                    last = nc.tensor.matmul(acc_wh[k % G][:, a % WB, :], xt[:, g % XT, a * P:(a + 1) * P],
                                            w_ext[:, :], start=True, stop=True)
                    if a % WB == WB - 1:
                        last.then_inc(wh_psum, 1)

            transpose_x(0)
            pe.wait_ge(wt_ready, 1)
            pe.wait_ge(a_in, 16)
            nc.tensor.matmul(acc[0][0][:, 0:2], wt[:, :], a_sb[:, :], start=True, stop=True).then_inc(wa_psum, 1)
            pe.wait_ge(wext_ready, 1)
            for g in range(NG):
                if g + 1 < NG:
                    transpose_x(g + 1)
                project_x(g)

            def pair(g, h, p, first, last, scaled=False):
                for k in range(PAIR):
                    if scaled and k % VC == 0:
                        pe.wait_ge(whv_ready, p * (PAIR // VC) + (k // VC + 1))
                    n = g * RT + p * PAIR + k
                    pe.wait_ge(pt_ready, n + 1)
                    for a in range(G):
                        if first and k == 0:
                            if not isinstance(g, int) or g >= H:
                                pe.wait_ge(acc_taken, (g - H) * G + (FIRST + a + 1))
                            elif g == 0:
                                pe.wait_ge(acc_taken, FIRST - G + a + 1)
                        mm = nc.tensor.matmul(
                            acc[h][a][:, 0:DE], pt[:, k % PR, a * P:(a + 1) * P],
                            whv[:, bass.ds(p * PAIR + k, 1), 0:DE].rearrange("p t d -> p (t d)"),
                            start=first and k == 0, stop=last and k == PAIR - 1)
                        if last and k == PAIR - 1:
                            mm.then_inc(acc_ready, 1)
                        elif a == G - 1:
                            mm.then_inc(pt_used, 1)

            pe.wait_ge(rhocol_ready, 1)
            for a in range(G):
                last = nc.tensor.transpose(rho_ps[:, a * P:(a + 1) * P],
                                           rho_col[:, a:a + 1].broadcast_to([P, P]), ident[:, :])
            last.then_inc(rho_psum, 1)
            pe.wait_ge(consts_ready, 1)
            nc.tensor.transpose(rho_t_ps[:, 0:P], rho_col[:, :], ident[:, :]).then_inc(rho_t_psum, 1)

            def group(n, h, scaled=False):
                g = n * H + h
                pair(g, h, 0, True, False, scaled)
                with pe.Fori(1, NP - 1) as p:
                    pair(g, h, p, False, False, scaled)
                pair(g, h, NP - 1, False, True, scaled)

            for h in range(H):
                group(0, h, scaled=h == 0)
            with pe.Fori(1, NS) as n:
                for h in range(H):
                    group(n, h)

            pe.wait_ge(wide_ready, 1)
            is_wide = pe.value_load(wide[0:1, 0:1], min_val=0, max_val=1)
            with pe.If(is_wide > 0):
                with pe.Fori(0, NG) as c:
                    pe.wait_ge(w_tnext_ready, c + 1)
                    for a in range(G):
                        last = nc.tensor.transpose(rho_ps[:, a * P:(a + 1) * P],
                                                   t_next[:, a:a + 1].broadcast_to([P, P]), ident[:, :])
                    last.then_inc(w_spread, 1)
                pe.wait_ge(w_x_in, 16)
                with pe.Fori(0, RT) as r:
                    pe.wait_ge(w_nums, r + 1)
                    for k in range(RT + 1):
                        if k < RT:
                            if k >= TR:
                                pe.wait_ge(w_copied, r * RT + (k - TR + 1))
                            nc.tensor.transpose(tr[k % TR][:, 0:P], e_row[:, k * P:(k + 1) * P],
                                                ident[:, :]).then_inc(w_tr, 1)
                        if k > 0:
                            pe.wait_ge(w_copied, r * RT + k)
                            nc.tensor.matmul(acc[0][0][:, 0:D], pt[:, (k - 1) % PR, 0:P],
                                             w_x[:, k - 1, :],
                                             start=k == 1, stop=k == RT).then_inc(w_mult, 1)
                    pe.wait_ge(w_px_ready, r + 1)
                    nc.tensor.transpose(tr[0][:, 0:P], w_px[:, :], ident[:, :]).then_inc(w_pxt_psum, 1)
                    pe.wait_ge(w_pxt_ready, r + 1)
                    nc.tensor.matmul(acc[0][1][:, 0:D], w_pxt[:, :], w_ext[:, 0:D],
                                     start=True, stop=True).then_inc(w_h, 1)


_INS = ["x", "adj", "L0_gnn_W", "L0_gnn_a"]
_OUTS = [((8192, 128), "float32")]


def kernel(**inputs):
    import numpy as _np
    import concourse.bacc as _bacc
    from concourse import mybir as _mybir
    from concourse.bass_utils import run_bass_kernel_spmd as _run

    nc = _bacc.Bacc("TRN2", target_bir_lowering=False, num_devices=1)
    arrays, args = {}, []
    for name in _INS:
        a = _np.ascontiguousarray(inputs[name])
        arrays[f"in_{name}_dram"] = a
        args.append(nc.dram_tensor(f"in_{name}_dram", a.shape, _mybir.dt.from_np(a.dtype), kind="ExternalInput").ap())
    for i, (shape, dtype) in enumerate(_OUTS):
        dt = _mybir.dt.from_np(_np.dtype(dtype))
        args.append(nc.dram_tensor(f"out_{i}_dram", shape, dt, kind="ExternalOutput").ap())
    gat_resnorm_kernel(nc, *args)
    r = _run(nc, [arrays], core_ids=[0])
    return r.results[0]["out_0_dram"]
```
